# Optimizing a Trainium2 kernel written in Bass

```python
import numpy as np
import jax
import jax.numpy as jnp

def _softmax(x, axis=-1):
    return jax.nn.softmax(x, axis=axis)

def _gelu(x):
    return jax.nn.gelu(x, approximate=True)

def _silu(x):
    return jax.nn.silu(x)

def _sigmoid(x):
    return jax.nn.sigmoid(x)

def _layernorm(x, axis=-1, eps=1e-05):
    m = jnp.mean(x, axis=axis, keepdims=True)
    v = jnp.var(x, axis=axis, keepdims=True)
    return (x - m) / jnp.sqrt(v + eps)

def _scatter_add(tgt, idx, src, axis=0):
    return tgt.at[idx].add(src)

def _segment_sum(src, seg, n):
    return jax.ops.segment_sum(src, seg, n)
kernel_name = 'mk_rec_standalone_d1_rec_r8_3f4f8d'

def setup_inputs(seed: int=0):
    np.random.seed(seed)
    _w = jnp.asarray

    def _rec_inputs():
        import jax
        import jax.numpy as jnp
        _rk = jax.random.key(seed)
        r_x = -0.00340659 + 1.00146 * jax.random.normal(jax.random.fold_in(_rk, 1), (2048, 64), jnp.float32)
        return r_x
    r_x = _rec_inputs()

    def _L0_rec_setup():
        import jax, jax.numpy as jnp
        import numpy as np
        SIGMA = 10.0
        EPS = 1e-10
        key = jax.random.key(seed)
        k1, k2, k3 = jax.random.split(key, 3)
        x = jax.random.normal(k1, (256, 64), dtype=jnp.float32)
        train_x = jax.random.normal(k2, (6250, 64), dtype=jnp.float32)
        train_y = jax.random.normal(k3, (6250, 16), dtype=jnp.float32)
        return {'x': x, 'train_x': train_x, 'train_y': train_y}
    _L0_rec_all = _L0_rec_setup()
    _L0_rec_in = {k: v for k, v in _L0_rec_all.items() if k in ('train_x', 'train_y')}
    del _L0_rec_all
    return {'r_x': r_x, 'L0_rec_train_x': _L0_rec_in['train_x'], 'L0_rec_train_y': _L0_rec_in['train_y']}

def reference(r_x, L0_rec_train_x, L0_rec_train_y):
    import jax
    import jax.numpy as jnp

    def _L0_rec_ref(x, train_x, train_y):
        import jax, jax.numpy as jnp
        import numpy as np
        SIGMA = 10.0
        EPS = 1e-10
        x_sq = jnp.sum(x * x, axis=1, keepdims=True)
        t_sq = jnp.sum(train_x * train_x, axis=1)
        cross = jnp.einsum('bd,nd->bn', x, train_x)
        distances = x_sq + t_sq[None, :] - 2.0 * cross
        weights = jnp.exp(-distances / (2.0 * SIGMA ** 2))
        normalized = weights / (jnp.sum(weights, axis=1, keepdims=True) + EPS)
        predictions = normalized @ train_y
        return predictions
    y = _L0_rec_ref(r_x, L0_rec_train_x, L0_rec_train_y)
    return y

_drawn_inputs = setup_inputs


def setup_inputs(seed=0):
    import zlib

    import numpy as np

    out = dict(_drawn_inputs(seed))
    spreads = {}
    factors = {}
    for name, (base, spread) in spreads.items():
        noise = np.random.default_rng([zlib.crc32(name.encode()), seed]).standard_normal(out[name].shape)
        drawn = base * np.exp(spread * noise) if base else spread * noise
        out[name] = jnp.asarray(drawn.astype(out[name].dtype))
    for name, factor in factors.items():
        out[name] = (out[name] * factor).astype(out[name].dtype)
    return out
```

```python
from contextlib import ExitStack

import concourse.bass as bass
from concourse import mybir

F32 = mybir.dt.float32
F32R = mybir.dt.float32r
ALU = mybir.AluOpType
ACT = mybir.ActivationFunctionType
AX_X = mybir.AxisListType.X

SIGMA = 10.0
EPS = 1e-10

P = 128
TILE = 512
YW = 32
RING = 3
STEP = 6


def build(nc, x_cols, t_cols, t_rows, y_rows, out):
    D2, B = x_cols.shape
    D = D2 // 2
    CHUNKS = t_rows.shape[1]
    TILES = B // TILE
    QT = TILE // P
    NY = out.shape[1]
    HALF = B // 2
    LAST = CHUNKS - 1
    LOOPS = LAST // STEP
    assert LAST % STEP == 0 and STEP % RING == 0 and TILES == 4 and 2 * D == P

    with ExitStack() as ctx:
        def sb(name, shape, dt=F32):
            return ctx.enter_context(nc.sbuf_tensor(name, shape, dt))

        def sem(name):
            return ctx.enter_context(nc.semaphore(name))

        x_raw = sb("x_raw", [P, B])
        tc_raw = sb("tc_raw", [P, CHUNKS * P])
        tr_raw = sb("tr_raw", [P, CHUNKS * D])
        y_raw = sb("y_raw", [P, CHUNKS * YW])
        x_first = sb("x_first", [P, B], F32R)
        x_second = sb("x_second", [P, B], F32R)
        x_square = sb("x_square", [D, B])
        neg_half = sb("neg_half", [D, D])
        t_first = sb("t_first", [P, RING, P], F32R)
        t_second = sb("t_second", [P, RING, P], F32R)
        y_ring = sb("y_ring", [P, RING, YW])
        t_square = sb("t_square", [P, D])
        bias = sb("bias", [P, RING])
        w = sb("w", [P, RING, B])
        sums_sb = sb("sums_sb", [P, TILE])
        ident = sb("ident", [P, P])
        denom = sb("denom", [P, TILES * QT])
        inv = sb("inv", [P, TILES * QT])
        result = sb("result", [P, TILES * QT * NY])

        units = [ctx.enter_context(nc.psum_tensor(f"unit{u}", [P, 2, TILE], F32)) for u in range(RING)]
        sums = ctx.enter_context(nc.psum_tensor("sums", [P, TILE], F32))
        turned = ctx.enter_context(nc.psum_tensor("turned", [P, QT, TILES, YW], F32))

        x_loaded = [sem(f"x_loaded{b}") for b in range(TILES)]
        cols_loaded, rows_loaded, y_loaded = sem("cols_loaded"), sem("rows_loaded"), sem("y_loaded")
        consts_ready = sem("consts_ready")
        ident_zeroed, ident_ready = sem("ident_zeroed"), sem("ident_ready")
        squares_ready = sem("squares_ready")
        norms_ready = sem("norms_ready")
        x_hi_ready = sem("x_hi_ready")
        norm_hi_ready = sem("norm_hi_ready")
        x_ready = sem("x_ready")
        t_hi_ready = sem("t_hi_ready")
        t_ready = sem("t_ready")
        t_squared = sem("t_squared")
        bias_ready = sem("bias_ready")
        y_ready = sem("y_ready")
        qk_done = sem("qk_done")
        exp_done = sem("exp_done")
        pv_done = sem("pv_done")
        sums_ready, turned_ready = sem("sums_ready"), sem("turned_ready")
        denom_ready, inv_ready, result_ready, stored = (
            sem("denom_ready"), sem("inv_ready"), sem("result_ready"), sem("stored"))

        bounds = [0, STEP // 2, STEP] + [STEP * (i + 1) for i in range(1, LOOPS)]
        bounds[-1] = CHUNKS
        PIECES = len(bounds) - 1

        def static(c):
            return c if isinstance(c, int) else None

        def norm_psum(b):
            return units[1 + b // 2][D:P, b % 2, :]

        def tile(a, b):
            return a[:, b * TILE:(b + 1) * TILE]

        block = ctx.enter_context(nc.Block())

        @block.sync
        def _(sp):
            def load_piece(i):
                a, b = bounds[i], bounds[i + 1]
                if i:
                    sp.wait_ge(cols_loaded, 16 * i)
                    sp.wait_ge(rows_loaded, 16 * i)
                    sp.wait_ge(y_loaded, 16 * i)
                sp.dma_start(tc_raw[:, a * P:b * P], t_cols[:, a * P:b * P]).then_inc(cols_loaded, 16)
                sp.dma_start(tr_raw[:, a * D:b * D], t_rows[:, a:b, :].rearrange("p c d -> p (c d)")
                             ).then_inc(rows_loaded, 16)
                sp.dma_start(y_raw[:, a * YW:b * YW], y_rows[:, a:b, :].rearrange("p c d -> p (c d)")
                             ).then_inc(y_loaded, 16)

            sp.dma_start(tile(x_raw, 0), tile(x_cols, 0)).then_inc(x_loaded[0], 16)
            sp.dma_start(tile(x_raw, 2), tile(x_cols, 2)).then_inc(x_loaded[2], 16)
            for i in range(PIECES):
                load_piece(i)
            sp.wait_ge(result_ready, 1)
            sp.dma_start(out.rearrange("(p m) y -> p (m y)", p=P), result[:, :]).then_inc(stored, 16)
            sp.wait_ge(stored, 16)

        @block.gpsimd
        def _(pool):
            nc.gpsimd.memset(neg_half[:, :], -0.5).then_inc(consts_ready, 1)
            pool.wait_ge(consts_ready, 1)
            nc.gpsimd.memset(t_second[D:P, :, :].bitcast(F32), 1.0 / 32).then_inc(consts_ready, 1)

            for c in range(STEP):
                if c in bounds:
                    pool.wait_ge(y_loaded, 16 * (bounds.index(c) + 1))
                if c >= RING:
                    pool.wait_ge(pv_done, c - (RING - 1))
                if c:
                    pool.wait_ge(y_ready, c)
                else:
                    pool.wait_ge(consts_ready, 2)
                nc.gpsimd.tensor_copy(y_ring[:, c % RING, :], y_raw[:, c * YW:(c + 1) * YW]).then_inc(y_ready, 1)
            pool.wait_ge(y_ready, STEP)
            nc.gpsimd.memset(ident[:, :], 0.0).then_inc(ident_zeroed, 1)
            pool.wait_ge(ident_zeroed, 1)
            nc.gpsimd.affine_select(out=ident[:, :], in_=ident[:, :], compare_op=ALU.not_equal, fill=1.0,
                                    base=0, pattern=[[-1, P]], channel_multiplier=1).then_inc(ident_ready, 1)
            pool.wait_ge(ident_ready, 1)
            with pool.Fori(1, LOOPS) as i:
                pool.wait_ge(y_loaded, 16 * i + 32)
                for k in range(STEP):
                    c = i * STEP + k
                    pool.wait_ge(pv_done, c - (RING - 1))
                    pool.wait_ge(y_ready, c)
                    nc.gpsimd.tensor_copy(y_ring[:, k % RING, :], y_raw[:, bass.ds(c * YW, YW)]
                                          ).then_inc(y_ready, 1)
            pool.wait_ge(pv_done, LAST - (RING - 1))
            pool.wait_ge(y_ready, LAST)
            nc.gpsimd.tensor_copy(y_ring[:, 0, :], y_raw[:, LAST * YW:CHUNKS * YW]).then_inc(y_ready, 1)

        @block.scalar
        def _(act):
            act.dma_start(tile(x_raw, 1), tile(x_cols, 1)).then_inc(x_loaded[1], 16)
            act.dma_start(tile(x_raw, 3), tile(x_cols, 3)).then_inc(x_loaded[3], 16)
            for b in range(TILES):
                act.wait_ge(x_loaded[b], 16)
                nc.scalar.activation(tile(x_square, b), tile(x_raw, b)[0:D], ACT.Square).then_inc(squares_ready, 1)

            def step(c, k, first=False):
                act.wait_ge(bias_ready, c + 1)
                if not first:
                    act.wait_ge(pv_done, c - (RING - 1))
                for h in range(2):
                    act.wait_ge(qk_done, 2 * c + h + 1)
                    nc.scalar.activation(w[:, k % RING, h * HALF:(h + 1) * HALF], units[(2 * k + h) % RING][:, :, :],
                                         ACT.Exp, bias=bias[:, k % RING:k % RING + 1],
                                         scale=1.0 / SIGMA ** 2).then_inc(exp_done, 1)

            for c in range(STEP):
                step(c, c, first=c < RING)
            with act.Fori(1, LOOPS) as i:
                for k in range(STEP):
                    step(i * STEP + k, k)
            step(LAST, 0)

        @block.vector
        def _(dve):
            def round_x(b):
                dve.wait_ge(x_loaded[b], 16)
                nc.vector.tensor_copy(tile(x_first, b), tile(x_raw, b)).then_inc(x_hi_ready, 1)
                dve.wait_ge(x_hi_ready, b + 1)
                nc.vector.tensor_tensor(tile(x_second, b)[0:D], tile(x_raw, b)[0:D], tile(x_first, b)[0:D],
                                        ALU.subtract)

            def round_norms(b):
                dve.wait_ge(norms_ready, b + 1)
                nc.vector.tensor_copy(tile(x_second, b)[D:P], norm_psum(b)).then_inc(norm_hi_ready, 1)
                dve.wait_ge(norm_hi_ready, b + 1)
                low = tile(x_second, b)[D + D // 2:P]
                nc.vector.tensor_tensor(low, units[1 + b // 2][D + D // 2:P, b % 2, :], low,
                                        ALU.subtract).then_inc(x_ready, 1)

            def step(c, k, first=False):
                cols = tc_raw[:, bass.ds(c * P, P)]
                rows = tr_raw[:, bass.ds(c * D, D)]
                s = k % RING
                if not first:
                    dve.wait_ge(exp_done, 2 * c - 2 * (RING - 1))
                nc.vector.tensor_copy(t_first[:, s, :], cols).then_inc(t_hi_ready, 1)
                nc.vector.tensor_copy(t_second[0:D, s, :], cols[0:D])
                dve.wait_ge(t_hi_ready, c + 1)
                nc.vector.tensor_tensor(t_first[D:P, s, :], cols[D:P], t_first[D:P, s, :],
                                        ALU.subtract).then_inc(t_ready, 1)
                if not first:
                    dve.wait_ge(bias_ready, c)
                nc.vector.scalar_tensor_tensor(out=t_square[:, :], in0=rows, scalar=-0.5 / SIGMA ** 2, in1=rows,
                                               op0=ALU.mult, op1=ALU.mult).then_inc(t_squared, 1)
                dve.wait_ge(t_squared, c + 1)
                nc.vector.tensor_reduce(bias[:, s:s + 1], t_square[:, :], AX_X, ALU.add).then_inc(bias_ready, 1)

            def wait_piece(n):
                dve.wait_ge(cols_loaded, n)
                dve.wait_ge(rows_loaded, n)

            round_x(0)
            wait_piece(16)
            step(0, 0, first=True)
            round_x(1)
            round_norms(0)
            round_norms(1)
            round_x(2)
            round_x(3)
            round_norms(2)
            round_norms(3)
            for c in range(1, STEP):
                if c in bounds:
                    wait_piece(16 * (bounds.index(c) + 1))
                step(c, c, first=c < RING)
            with dve.Fori(1, LOOPS) as i:
                wait_piece(16 * i + 32)
                for k in range(STEP):
                    step(i * STEP + k, k)
            step(LAST, 0)

            dve.wait_ge(pv_done, CHUNKS)
            nc.vector.tensor_copy(sums_sb[:, :], sums[:, :]).then_inc(sums_ready, 1)
            dve.wait_ge(turned_ready, 1)
            by_block = turned[:, :, :, :].rearrange("p i j y -> p j i y")
            wide = "p (j i) -> p j i"
            nc.vector.tensor_scalar(denom[:, :].rearrange(wide, j=TILES), by_block[:, :, :, NY], EPS, None,
                                    ALU.add).then_inc(denom_ready, 1)
            dve.wait_ge(denom_ready, 1)
            nc.vector.reciprocal(inv[:, :], denom[:, :]).then_inc(inv_ready, 1)
            dve.wait_ge(inv_ready, 1)
            res = result[:, :].rearrange("p (j i y) -> p j i y", j=TILES, i=QT)
            iv = inv[:, :].rearrange(wide, j=TILES)
            for j in range(TILES):
                last = nc.vector.tensor_tensor(res[:, j], by_block[:, j, :, 0:NY],
                                               iv[:, j].unsqueeze(2).to_broadcast([P, QT, NY]), ALU.mult)
            last.then_inc(result_ready, 1)

        @block.tensor
        def _(pe):
            pe.wait_ge(consts_ready, 2)
            for b in range(TILES):
                pe.wait_ge(squares_ready, b + 1)
                nc.tensor.matmul(norm_psum(b), neg_half[:, :], tile(x_square, b), start=True, stop=True
                                 ).then_inc(norms_ready, 1)

            def exponents(c, k, first=False):
                pe.wait_ge(t_ready, c + 1)
                for h in range(2):
                    unit = units[(2 * k + h) % RING]
                    if not first:
                        pe.wait_ge(exp_done, 2 * c + h - (RING - 1))
                    for q in range(2):
                        if static(c) == 0:
                            if h == 1:
                                pe.wait_ge(x_ready, 2)
                            pe.wait_ge(x_hi_ready, 2 * h + q + 1)
                        nc.tensor.matmul(unit[:, q, :], t_first[:, k % RING, :], tile(x_first, 2 * h + q),
                                         start=True, stop=False)
                    for q in range(2):
                        if static(c) == 0:
                            pe.wait_ge(x_ready, 2 * h + q + 1)
                        mm = nc.tensor.matmul(unit[:, q, :], t_second[:, k % RING, :], tile(x_second, 2 * h + q),
                                              start=False, stop=True)
                    mm.then_inc(qk_done, 1)

            def products(c, k, start=False, stop=False):
                pe.wait_ge(y_ready, c + 1)
                pe.wait_ge(exp_done, 2 * c + 2)
                for j in range(TILES):
                    mm = nc.tensor.matmul(sums[j * YW:(j + 1) * YW, :], y_ring[:, k % RING, :],
                                          w[:, k % RING, j * TILE:(j + 1) * TILE], start=start, stop=stop)
                mm.then_inc(pv_done, 1)

            def step(c, k, first=False):
                exponents(c, k, first)
                products(c - 1, (k - 1) % STEP, start=static(c) == 1)

            exponents(0, 0, first=True)
            for c in range(1, STEP):
                step(c, c, first=False)
            with pe.Fori(1, LOOPS) as i:
                for k in range(STEP):
                    step(i * STEP + k, k)
            step(LAST, 0)
            products(LAST, 0, stop=True)

            pe.wait_ge(ident_ready, 1)
            pe.wait_ge(sums_ready, 1)
            for i in range(QT):
                mm = nc.tensor.transpose(turned[:, i, :, :].rearrange("p j y -> p (j y)"),
                                         sums_sb[:, i * P:(i + 1) * P], ident[:, :])
            mm.then_inc(turned_ready, 1)


def kernel(r_x, L0_rec_train_x, L0_rec_train_y):
    import numpy as np
    import concourse.bacc as bacc
    from concourse.bass_utils import run_bass_kernel_spmd

    x, t, y = np.asarray(r_x), np.asarray(L0_rec_train_x), np.asarray(L0_rec_train_y)
    (B, D), (N, NY) = x.shape, y.shape
    chunks = -(-N // P)
    x_cols = x.reshape(P, B // P, D).transpose(2, 1, 0).reshape(D, B)
    x_cols = np.concatenate([x_cols, x_cols])
    t_pad = np.zeros((chunks * P, D), t.dtype)
    t_pad[:N] = t
    t_cols = np.concatenate([t_pad.T, t_pad.T])
    t_rows = t_pad.reshape(chunks, P, D).transpose(1, 0, 2)
    y_pad = np.zeros((chunks * P, YW), y.dtype)
    y_pad[:N, :NY] = y
    y_pad[:N, NY] = 1.0
    y_rows = y_pad.reshape(chunks, P, YW).transpose(1, 0, 2)

    nc = bacc.Bacc("TRN2", target_bir_lowering=False, num_devices=1)
    arrays, args = {}, []
    for name, a in (("x_cols", x_cols), ("t_cols", t_cols), ("t_rows", t_rows), ("y_rows", y_rows)):
        arrays[name] = np.ascontiguousarray(a)
        args.append(nc.dram_tensor(name, a.shape, mybir.dt.from_np(a.dtype), kind="ExternalInput").ap())
    out = nc.dram_tensor("out", (B, NY), F32, kind="ExternalOutput").ap()
    build(nc, *args, out)
    r = run_bass_kernel_spmd(nc, [arrays], core_ids=[0])
    return r.results[0]["out"]
```

```python
from contextlib import ExitStack

import concourse.bass as bass
from concourse import mybir

F32 = mybir.dt.float32
F32R = mybir.dt.float32r
BF16 = mybir.dt.bfloat16
ALU = mybir.AluOpType
ACT = mybir.ActivationFunctionType
AX_X = mybir.AxisListType.X

SIGMA = 10.0
EPS = 1e-10

P = 128
TILE = 512
YW = 32
GROUP = 3
UNITS = 3
RING = 2 * GROUP
PER_GROUP = 2 * GROUP
POOL_CHUNKS = GROUP - 1
WARM_UPS = 7


def build(nc, x_cols, t_cols, rows, out):
    D = x_cols.shape[0] // 2
    B = x_cols.shape[1]
    CHUNKS, ROW = rows.shape[1:]
    TILES = B // TILE
    QT = TILE // P
    NY = out.shape[1]
    HALF = B // 2
    LAST = CHUNKS - 1
    GROUPS = LAST // GROUP
    LOOPS = LAST // RING
    assert LAST % RING == 0 and PER_GROUP % UNITS == 0 and TILES == 4 and 2 * D == P and ROW == D + YW

    with ExitStack() as ctx:
        def sb(name, shape, dt=F32):
            return ctx.enter_context(nc.sbuf_tensor(name, shape, dt))

        def sem(name):
            return ctx.enter_context(nc.semaphore(name))

        x_raw = sb("x_raw", [P, B])
        cols_raw = sb("cols_raw", [P, CHUNKS * P])
        rows_raw = sb("rows_raw", [P, CHUNKS * ROW])
        x_first = sb("x_first", [P, B], F32R)
        x_second = sb("x_second", [P, B], F32R)
        x_square = sb("x_square", [D, B])
        neg_half = sb("neg_half", [D, YW])
        zeros = sb("zeros", [P, P], BF16)
        t_first = sb("t_first", [P, RING, P], F32R)
        t_second = sb("t_second", [P, RING, P], F32R)
        y_ring = sb("y_ring", [P, RING, YW])
        t_square = sb("t_square", [P, D])
        bias = sb("bias", [P, RING])
        w = sb("w", [P, RING, B])
        sums_sb = sb("sums_sb", [P, TILE])
        ident = sb("ident", [P, P])
        denom = sb("denom", [P, TILES * QT])
        inv = sb("inv", [P, TILES * QT])
        result = sb("result", [P, TILES * QT * NY])

        units = [ctx.enter_context(nc.psum_tensor(f"unit{u}", [P, 2, TILE], F32)) for u in range(UNITS)]
        sums = ctx.enter_context(nc.psum_tensor("sums", [P, TILE], F32))
        turned = ctx.enter_context(nc.psum_tensor("turned", [P, QT, TILES, YW], F32))

        x_loaded = [sem(f"x_loaded{b}") for b in range(TILES)]
        cols_loaded, rows_loaded = sem("cols_loaded"), sem("rows_loaded")
        consts_ready, zeros_ready = sem("consts_ready"), sem("zeros_ready")
        ident_zeroed, ident_ready = sem("ident_zeroed"), sem("ident_ready")
        squares_ready = sem("squares_ready")
        norms_ready = sem("norms_ready")
        norm_hi_ready = sem("norm_hi_ready")
        norm_lo_ready = sem("norm_lo_ready")
        x_hi_ready = sem("x_hi_ready")
        x_lo_ready = sem("x_lo_ready")
        x_lo_pool = sem("x_lo_pool")
        t_hi_ready = sem("t_hi_ready")
        t_ready = sem("t_ready")
        t_pool = sem("t_pool")
        t_squared = sem("t_squared")
        bias_ready = sem("bias_ready")
        y_ready = sem("y_ready")
        products_done = sem("products_done")
        exponents_ready = sem("exponents_ready")
        weights_ready = sem("weights_ready")
        sums_ready, turned_ready = sem("sums_ready"), sem("turned_ready")
        denom_ready, inv_ready, result_ready, stored = (
            sem("denom_ready"), sem("inv_ready"), sem("result_ready"), sem("stored"))

        bounds = [0, GROUP] + [RING * i for i in range(1, LOOPS)] + [CHUNKS]
        AHEAD = bounds.index(RING) - 1

        def tile(a, b):
            return a[:, b * TILE:(b + 1) * TILE]

        block = ctx.enter_context(nc.Block())

        @block.sync
        def _(sp):
            def load_cols(i):
                a, b = bounds[i], bounds[i + 1]
                if i:
                    sp.wait_ge(cols_loaded, 16 * i)
                sp.dma_start(cols_raw[:, a * P:b * P], t_cols[:, a * P:b * P]).then_inc(cols_loaded, 16)

            def load_rows(i):
                a, b = bounds[i], bounds[i + 1]
                if i:
                    sp.wait_ge(rows_loaded, 16 * i)
                sp.dma_start(rows_raw[:, a * ROW:b * ROW], rows[:, a:b, :].rearrange("p c d -> p (c d)")
                             ).then_inc(rows_loaded, 16)

            def load_x(b):
                sp.dma_start(tile(x_raw, b), tile(x_cols, b)).then_inc(x_loaded[b], 16)

            load_x(0)
            load_cols(0)
            load_x(1)
            load_x(2)
            load_rows(0)
            load_x(3)
            for i in range(1, len(bounds) - 1):
                load_cols(i)
                load_rows(i)
            sp.wait_ge(result_ready, 1)
            sp.dma_start(out.rearrange("(p m) y -> p (m y)", p=P), result[:, :]).then_inc(stored, 16)
            sp.wait_ge(stored, 16)

        @block.gpsimd
        def _(pool):
            nc.gpsimd.memset(neg_half[:, :], -0.5).then_inc(consts_ready, 1)
            pool.wait_ge(consts_ready, 1)
            nc.gpsimd.memset(t_second[D:P, :, :].bitcast(F32), 1.0 / 32).then_inc(consts_ready, 1)
            pool.wait_ge(consts_ready, 2)

            def copy_y(c, k, first=False):
                if not first:
                    pool.wait_ge(products_done, c - (RING - 1))
                nc.gpsimd.tensor_copy(y_ring[:, k, :], rows_raw[:, bass.ds(c * ROW + D, YW)]).then_inc(y_ready, 1)
                pool.wait_ge(y_ready, c + 1)

            pool.wait_ge(cols_loaded, 16)
            for c in range(1, GROUP):
                cols = cols_raw[:, c * P:(c + 1) * P]
                nc.gpsimd.tensor_copy(t_first[:, c, :], cols).then_inc(t_pool, 1)
                pool.wait_ge(t_pool, 3 * c - 2)
                nc.gpsimd.tensor_copy(t_second[0:D, c, :], cols[0:D]).then_inc(t_pool, 1)
                pool.wait_ge(t_pool, 3 * c - 1)
                nc.gpsimd.tensor_tensor(t_first[D:P, c, :], cols[D:P], t_first[D:P, c, :],
                                        ALU.subtract).then_inc(t_pool, 1)
                pool.wait_ge(t_pool, 3 * c)

            for b in range(2, TILES):
                pool.wait_ge(x_hi_ready, b + 1)
                nc.gpsimd.tensor_tensor(tile(x_second, b)[0:D], tile(x_raw, b)[0:D], tile(x_first, b)[0:D],
                                        ALU.subtract).then_inc(x_lo_pool, 1)
                pool.wait_ge(x_lo_pool, b - 1)

            for c in range(RING):
                if c in bounds:
                    pool.wait_ge(rows_loaded, 16 * (bounds.index(c) + 1))
                copy_y(c, c, first=True)
            nc.gpsimd.memset(ident[:, :], 0.0).then_inc(ident_zeroed, 1)
            pool.wait_ge(ident_zeroed, 1)
            nc.gpsimd.affine_select(out=ident[:, :], in_=ident[:, :], compare_op=ALU.not_equal, fill=1.0,
                                    base=0, pattern=[[-1, P]], channel_multiplier=1).then_inc(ident_ready, 1)
            pool.wait_ge(ident_ready, 1)
            with pool.Fori(1, LOOPS) as i:
                pool.wait_ge(rows_loaded, 16 * i + 16 * (AHEAD + 1))
                for k in range(RING):
                    copy_y(i * RING + k, k)
            copy_y(LAST, 0)

        @block.scalar
        def _(act):
            def square(b):
                act.wait_ge(x_loaded[b], 16)
                nc.scalar.activation(tile(x_square, b), tile(x_raw, b)[0:D], ACT.Square).then_inc(squares_ready, 1)

            def norm_hi(b):
                act.wait_ge(norms_ready, b + 1)
                nc.scalar.activation(tile(x_second, b)[D:D + YW], sums[b * YW:(b + 1) * YW, :], ACT.Copy
                                     ).then_inc(norm_hi_ready, 1)

            square(0)
            square(1)
            norm_hi(0)
            norm_hi(1)
            square(2)
            square(3)
            norm_hi(2)
            norm_hi(3)

            def weights(u, k, h, pos):
                act.wait_ge(exponents_ready, u + 1)
                nc.scalar.activation(w[:, k, h * HALF:(h + 1) * HALF], units[pos % UNITS][:, :, :], ACT.Exp,
                                     bias=bias[:, k:k + 1], scale=1.0 / SIGMA ** 2).then_inc(weights_ready, 1)

            def group(g, half, first=False):
                for h in range(2):
                    for r in range(GROUP):
                        if h == 0:
                            act.wait_ge(bias_ready, g * GROUP + r + 1)
                            if not first:
                                act.wait_ge(products_done, g * GROUP + r - (RING - 1))
                        pos = h * GROUP + r
                        weights(g * PER_GROUP + pos, half * GROUP + r, h, pos)

            group(0, 0, first=True)
            group(1, 1, first=True)
            with act.Fori(1, LOOPS) as i:
                group(2 * i, 0)
                group(2 * i + 1, 1)
            act.wait_ge(bias_ready, CHUNKS)
            act.wait_ge(products_done, LAST - (RING - 1))
            for h in range(2):
                weights(2 * LAST + h, 0, h, h)

        @block.vector
        def _(dve):
            def x_hi(b):
                dve.wait_ge(x_loaded[b], 16)
                nc.vector.tensor_copy(tile(x_first, b), tile(x_raw, b)).then_inc(x_hi_ready, 1)

            def x_lo(b):
                dve.wait_ge(x_hi_ready, b + 1)
                nc.vector.tensor_tensor(tile(x_second, b)[0:D], tile(x_raw, b)[0:D], tile(x_first, b)[0:D],
                                        ALU.subtract).then_inc(x_lo_ready, 1)

            def norm_lo(b):
                dve.wait_ge(norm_hi_ready, b + 1)
                nc.vector.tensor_tensor(tile(x_second, b)[D + YW:P], sums[b * YW:(b + 1) * YW, :],
                                        tile(x_second, b)[D:D + YW], ALU.subtract).then_inc(norm_lo_ready, 1)

            def operands(c, k):
                made = c + 1 if isinstance(c, int) and c == 0 else c + 1 - POOL_CHUNKS
                cols = cols_raw[:, bass.ds(c * P, P)]
                nc.vector.tensor_copy(t_first[:, k, :], cols).then_inc(t_hi_ready, 1)
                nc.vector.tensor_copy(t_second[0:D, k, :], cols[0:D])
                dve.wait_ge(t_hi_ready, made)
                nc.vector.tensor_tensor(t_first[D:P, k, :], cols[D:P], t_first[D:P, k, :],
                                        ALU.subtract).then_inc(t_ready, 1)

            def make_bias(c, k, first=False):
                t = rows_raw[:, bass.ds(c * ROW, D)]
                if not first:
                    dve.wait_ge(bias_ready, c)
                nc.vector.scalar_tensor_tensor(out=t_square[:, :], in0=t, scalar=-0.5 / SIGMA ** 2, in1=t,
                                               op0=ALU.mult, op1=ALU.mult).then_inc(t_squared, 1)
                dve.wait_ge(t_squared, c + 1)
                nc.vector.tensor_reduce(bias[:, k:k + 1], t_square[:, :], AX_X, ALU.add).then_inc(bias_ready, 1)

            def wait_piece(n):
                dve.wait_ge(cols_loaded, n)
                dve.wait_ge(rows_loaded, n)

            nc.vector.memset(zeros[:, :], 0.0).then_inc(zeros_ready, 1)
            x_hi(0)
            x_lo(0)
            dve.wait_ge(cols_loaded, 16)
            operands(0, 0)
            x_hi(1)
            x_lo(1)
            dve.wait_ge(rows_loaded, 16)
            make_bias(0, 0, first=True)
            make_bias(1, 1)
            norm_lo(0)
            norm_lo(1)
            x_hi(2)
            x_hi(3)
            make_bias(2, 2)
            norm_lo(2)
            norm_lo(3)
            wait_piece(32)
            for c in range(GROUP, RING):
                operands(c, c)
                make_bias(c, c)

            def group(g, half):
                dve.wait_ge(weights_ready, g * PER_GROUP - PER_GROUP)
                for r in range(GROUP):
                    operands(g * GROUP + r, half * GROUP + r)
                    make_bias(g * GROUP + r, half * GROUP + r)

            with dve.Fori(1, LOOPS) as i:
                wait_piece(16 * i + 16 * (AHEAD + 1))
                group(2 * i, 0)
                group(2 * i + 1, 1)
            dve.wait_ge(weights_ready, (GROUPS - 1) * PER_GROUP)
            operands(LAST, 0)
            make_bias(LAST, 0)

            dve.wait_ge(products_done, CHUNKS)
            nc.vector.tensor_copy(sums_sb[:, :], sums[:, :]).then_inc(sums_ready, 1)
            dve.wait_ge(turned_ready, 1)
            by_tile = turned[:, :, :, :].rearrange("p i j y -> p j i y")
            grid = "p (j i) -> p j i"
            nc.vector.tensor_scalar(denom[:, :].rearrange(grid, j=TILES), by_tile[:, :, :, NY], EPS, None,
                                    ALU.add).then_inc(denom_ready, 1)
            dve.wait_ge(denom_ready, 1)
            nc.vector.reciprocal(inv[:, :], denom[:, :]).then_inc(inv_ready, 1)
            dve.wait_ge(inv_ready, 1)
            nc.vector.tensor_tensor(result[:, :].rearrange("p (j i y) -> p j i y", j=TILES, i=QT),
                                    by_tile[:, :, :, 0:NY],
                                    inv[:, :].rearrange(grid, j=TILES).unsqueeze(3).to_broadcast([P, TILES, QT, NY]),
                                    ALU.mult).then_inc(result_ready, 1)

        @block.tensor
        def _(pe):
            def norms(b):
                pe.wait_ge(squares_ready, b + 1)
                nc.tensor.matmul(sums[b * YW:(b + 1) * YW, :], neg_half[:, :], tile(x_square, b),
                                 start=True, stop=True).then_inc(norms_ready, 1)

            def first_pass(k, h, pos, wait_x=False):
                for q in range(2):
                    if wait_x:
                        pe.wait_ge(x_hi_ready, 2 * h + q + 1)
                    nc.tensor.matmul(units[pos % UNITS][:, q, :], t_first[:, k, :], tile(x_first, 2 * h + q),
                                     start=True, stop=False)

            def second_pass(k, h, pos, wait_x=False):
                for q in range(2):
                    if wait_x:
                        pe.wait_ge(x_lo_pool if h else x_lo_ready, q + 1)
                        pe.wait_ge(norm_lo_ready, 2 * h + q + 1)
                    mm = nc.tensor.matmul(units[pos % UNITS][:, q, :], t_second[:, k, :],
                                          tile(x_second, 2 * h + q), start=False, stop=True)
                mm.then_inc(exponents_ready, 1)

            def exponents(u, k, h, pos, wait_x=False):
                pe.wait_ge(weights_ready, u - (UNITS - 1))
                first_pass(k, h, pos, wait_x)
                second_pass(k, h, pos, wait_x)

            def products(c, k, start=False, stop=False):
                pe.wait_ge(y_ready, c + 1)
                for j in range(TILES):
                    mm = nc.tensor.matmul(sums[j * YW:(j + 1) * YW, :], y_ring[:, k, :],
                                          w[:, k, j * TILE:(j + 1) * TILE], start=start, stop=stop)
                mm.then_inc(products_done, 1)

            def group_exponents(g, half):
                for h in range(2):
                    for r in range(GROUP):
                        if h == 0:
                            pe.wait_ge(t_ready, g * GROUP + r + 1 - POOL_CHUNKS)
                        pos = h * GROUP + r
                        exponents(g * PER_GROUP + pos, half * GROUP + r, h, pos)

            def group_products(g, half, start=False):
                for r in range(GROUP):
                    pe.wait_ge(weights_ready, g * PER_GROUP + GROUP + r + 1)
                    products(g * GROUP + r, half * GROUP + r, start=start and r == 0)

            pe.wait_ge(zeros_ready, 1)
            for _ in range(WARM_UPS):
                nc.tensor.matmul(units[0][:, 0, :], zeros[:, :],
                                 zeros[:, :].unsqueeze(1).to_broadcast([P, TILE // P, P]), start=True, stop=True)
            pe.wait_ge(consts_ready, 2)
            norms(0)
            norms(1)
            pe.wait_ge(t_ready, 1)
            first_pass(0, 0, 0, wait_x=True)
            pe.wait_ge(t_pool, 3)
            first_pass(1, 0, 1)
            norms(2)
            second_pass(0, 0, 0, wait_x=True)
            norms(3)
            second_pass(1, 0, 1)
            pe.wait_ge(t_pool, 6)
            first_pass(2, 0, 2)
            second_pass(2, 0, 2)
            for r in range(GROUP):
                exponents(GROUP + r, r, 1, GROUP + r, wait_x=r == 0)
            group_exponents(1, 1)
            group_products(0, 0, start=True)
            with pe.Fori(1, LOOPS) as i:
                group_exponents(2 * i, 0)
                group_products(2 * i - 1, 1)
                group_exponents(2 * i + 1, 1)
                group_products(2 * i, 0)
            pe.wait_ge(t_ready, CHUNKS - POOL_CHUNKS)
            for h in range(2):
                exponents(2 * LAST + h, 0, h, h)
            group_products(GROUPS - 1, 1)
            pe.wait_ge(weights_ready, 2 * CHUNKS)
            products(LAST, 0, stop=True)

            pe.wait_ge(ident_ready, 1)
            pe.wait_ge(sums_ready, 1)
            for i in range(QT):
                mm = nc.tensor.transpose(turned[:, i, :, :].rearrange("p j y -> p (j y)"),
                                         sums_sb[:, i * P:(i + 1) * P], ident[:, :])
            mm.then_inc(turned_ready, 1)


def kernel(r_x, L0_rec_train_x, L0_rec_train_y):
    import numpy as np
    import concourse.bacc as bacc
    from concourse.bass_utils import run_bass_kernel_spmd

    x, t, y = np.asarray(r_x), np.asarray(L0_rec_train_x), np.asarray(L0_rec_train_y)
    (B, D), (N, NY) = x.shape, y.shape
    chunks = -(-N // P)
    x_cols = x.reshape(P, B // P, D).transpose(2, 1, 0).reshape(D, B)
    x_cols = np.concatenate([x_cols, x_cols])
    t_pad = np.zeros((chunks * P, D), t.dtype)
    t_pad[:N] = t
    t_cols = np.concatenate([t_pad.T, t_pad.T])
    rows = np.zeros((chunks * P, D + YW), t.dtype)
    rows[:N, :D] = t
    rows[:N, D:D + NY] = y
    rows[:N, D + NY] = 1.0
    rows = rows.reshape(chunks, P, D + YW).transpose(1, 0, 2)

    nc = bacc.Bacc("TRN2", target_bir_lowering=False, num_devices=1)
    arrays, args = {}, []
    for name, a in (("x_cols", x_cols), ("t_cols", t_cols), ("rows", rows)):
        arrays[name] = np.ascontiguousarray(a)
        args.append(nc.dram_tensor(name, a.shape, mybir.dt.from_np(a.dtype), kind="ExternalInput").ap())
    out = nc.dram_tensor("out", (B, NY), F32, kind="ExternalOutput").ap()
    build(nc, *args, out)
    r = run_bass_kernel_spmd(nc, [arrays], core_ids=[0])
    return r.results[0]["out"]
```
